# Optimizing a Trainium2 kernel written in Bass

```python
import numpy as np
import jax
import jax.numpy as jnp

def _softmax(x, axis=-1):
    return jax.nn.softmax(x, axis=axis)

def _gelu(x):
    return jax.nn.gelu(x, approximate=True)

def _silu(x):
    return jax.nn.silu(x)

def _sigmoid(x):
    return jax.nn.sigmoid(x)

def _layernorm(x, axis=-1, eps=1e-05):
    m = jnp.mean(x, axis=axis, keepdims=True)
    v = jnp.var(x, axis=axis, keepdims=True)
    return (x - m) / jnp.sqrt(v + eps)

def _scatter_add(tgt, idx, src, axis=0):
    return tgt.at[idx].add(src)

def _segment_sum(src, seg, n):
    return jax.ops.segment_sum(src, seg, n)
kernel_name = 'mk_adj_resnorm_d2_adj_r2_01f607'

def setup_inputs(seed: int=0):
    np.random.seed(seed)
    _w = jnp.asarray

    def _rec_inputs():
        import jax
        import jax.numpy as jnp
        _gk = jax.random.key(seed)
        x = -1.394e-06 + 0.9999 * jax.random.normal(jax.random.fold_in(_gk, 1), (4096, 256), jnp.float32)
        _a = jax.random.bernoulli(jax.random.fold_in(_gk, 2), 0.000488281, (4096, 4096))
        _a = jnp.logical_or(_a, jnp.swapaxes(_a, -1, -2))
        _a = jnp.logical_or(_a, jnp.eye(4096, dtype=bool))
        adj = _a
        return (x, adj)
    x, adj = _rec_inputs()

    def _L0_gnn_setup():
        import jax, jax.numpy as jnp
        import numpy as np
        import math
        N = 4096
        D_IN = 256
        LOCAL_D = 256
        GLOBAL_D = 256
        key = jax.random.key(seed)
        ks = jax.random.split(key, 16)
        s = 1.0 / math.sqrt(D_IN)
        adj = jax.random.bernoulli(ks[0], 0.01, (N, N))
        adj = adj | jnp.eye(N, dtype=bool)
        return {'adj_matrix': adj, 'x': jax.random.normal(ks[1], (N, D_IN), jnp.float32), 'masked_x': jax.random.normal(ks[2], (N, D_IN), jnp.float32), 'Wlq': jax.random.normal(ks[3], (D_IN, LOCAL_D), jnp.float32) * s, 'Wlk': jax.random.normal(ks[4], (D_IN, LOCAL_D), jnp.float32) * s, 'Wlv': jax.random.normal(ks[5], (D_IN, D_IN), jnp.float32) * s, 'blv': jax.random.normal(ks[6], (D_IN,), jnp.float32) * 0.01, 'Wgq': jax.random.normal(ks[7], (D_IN, GLOBAL_D), jnp.float32) * s, 'Wgk': jax.random.normal(ks[8], (D_IN, GLOBAL_D), jnp.float32) * s, 'Wgv': jax.random.normal(ks[9], (D_IN, D_IN), jnp.float32) * s, 'bgv': jax.random.normal(ks[10], (D_IN,), jnp.float32) * 0.01, 'Wes': jax.random.normal(ks[11], (D_IN, 1), jnp.float32) * s, 'Wev': jax.random.normal(ks[12], (D_IN, D_IN), jnp.float32) * s, 'bev': jax.random.normal(ks[13], (D_IN,), jnp.float32) * 0.01}
    _L0_gnn_all = _L0_gnn_setup()
    _L0_gnn_in = {k: v for k, v in _L0_gnn_all.items() if k in ('masked_x', 'Wlq', 'Wlk', 'Wlv', 'blv', 'Wgq', 'Wgk', 'Wgv', 'bgv', 'Wes', 'Wev', 'bev')}
    del _L0_gnn_all

    def _L1_gnn_setup():
        import jax, jax.numpy as jnp
        import numpy as np
        N = 4096
        D = 256
        NEG = -1e+30
        key = jax.random.key(seed)
        ks = jax.random.split(key, 5)
        neuron_states = jax.random.normal(ks[0], (N, D), dtype=jnp.float32)
        adjacency = jax.random.bernoulli(ks[1], 0.05, (N, N))
        Wq = jax.random.normal(ks[2], (D, D), dtype=jnp.float32) / np.sqrt(D)
        Wk = jax.random.normal(ks[3], (D, D), dtype=jnp.float32) / np.sqrt(D)
        Wv = jax.random.normal(ks[4], (D, D), dtype=jnp.float32) / np.sqrt(D)
        return {'neuron_states': neuron_states, 'adjacency': adjacency, 'Wq': Wq, 'Wk': Wk, 'Wv': Wv}
    _L1_gnn_all = _L1_gnn_setup()
    _L1_gnn_in = {k: v for k, v in _L1_gnn_all.items() if k in ('Wq', 'Wk', 'Wv')}
    del _L1_gnn_all
    return {'x': x, 'adj': adj, 'L0_gnn_masked_x': _L0_gnn_in['masked_x'], 'L0_gnn_Wlq': _L0_gnn_in['Wlq'], 'L0_gnn_Wlk': _L0_gnn_in['Wlk'], 'L0_gnn_Wlv': _L0_gnn_in['Wlv'], 'L0_gnn_blv': _L0_gnn_in['blv'], 'L0_gnn_Wgq': _L0_gnn_in['Wgq'], 'L0_gnn_Wgk': _L0_gnn_in['Wgk'], 'L0_gnn_Wgv': _L0_gnn_in['Wgv'], 'L0_gnn_bgv': _L0_gnn_in['bgv'], 'L0_gnn_Wes': _L0_gnn_in['Wes'], 'L0_gnn_Wev': _L0_gnn_in['Wev'], 'L0_gnn_bev': _L0_gnn_in['bev'], 'L1_gnn_Wq': _L1_gnn_in['Wq'], 'L1_gnn_Wk': _L1_gnn_in['Wk'], 'L1_gnn_Wv': _L1_gnn_in['Wv']}

def reference(x, adj, L0_gnn_masked_x, L0_gnn_Wlq, L0_gnn_Wlk, L0_gnn_Wlv, L0_gnn_blv, L0_gnn_Wgq, L0_gnn_Wgk, L0_gnn_Wgv, L0_gnn_bgv, L0_gnn_Wes, L0_gnn_Wev, L0_gnn_bev, L1_gnn_Wq, L1_gnn_Wk, L1_gnn_Wv):
    import jax
    import jax.numpy as jnp

    def _L0_gnn_ref(adj_matrix, x, masked_x, Wlq, Wlk, Wlv, blv, Wgq, Wgk, Wgv, bgv, Wes, Wev, bev):
        import jax, jax.numpy as jnp
        import numpy as np
        import math
        N = 4096
        D_IN = 256
        LOCAL_D = 256
        GLOBAL_D = 256
        scale = 1.0 / math.sqrt(D_IN)
        x_bar = jnp.mean(x, axis=0, keepdims=True)
        lQ = masked_x @ Wlq
        lK = x @ Wlk
        lV = x @ Wlv + blv
        gQ = masked_x @ Wgq
        gK = x_bar @ Wgk
        gV = x_bar @ Wgv + bgv
        es = masked_x @ Wes
        eV = masked_x @ Wev + bev
        local_scores = lQ @ lK.T * scale
        local_scores = jnp.where(adj_matrix, local_scores, jnp.float32(-1000000000.0))
        global_scores = gQ @ gK.T * scale
        max_score = jnp.maximum(jnp.max(local_scores, axis=1, keepdims=True), jnp.maximum(global_scores, es))
        le = jnp.exp(local_scores - max_score)
        ge = jnp.exp(global_scores - max_score)
        ee = jnp.exp(es - max_score)
        denom = jnp.sum(le, axis=-1, keepdims=True) + ge + ee
        res = le / denom @ lV + ge / denom * gV + ee / denom * eV
        x_recon = jnp.maximum(res, masked_x)
        return x_recon

    def _L1_gnn_ref(neuron_states, adjacency, Wq, Wk, Wv):
        import jax, jax.numpy as jnp
        import numpy as np
        N = 4096
        D = 256
        NEG = -1e+30
        q = neuron_states @ Wq.T
        k = neuron_states @ Wk.T
        v = neuron_states @ Wv.T
        mask = adjacency.T
        scores = jnp.where(mask, q @ k.T, NEG)
        attn = jax.nn.softmax(scores, axis=1)
        attn = jnp.where(mask, attn, 0.0)
        return attn @ v
    x = _layernorm(x + _L0_gnn_ref(adj, x, L0_gnn_masked_x, L0_gnn_Wlq, L0_gnn_Wlk, L0_gnn_Wlv, L0_gnn_blv, L0_gnn_Wgq, L0_gnn_Wgk, L0_gnn_Wgv, L0_gnn_bgv, L0_gnn_Wes, L0_gnn_Wev, L0_gnn_bev), axis=-1)
    x = _layernorm(x + _L1_gnn_ref(x, adj, L1_gnn_Wq, L1_gnn_Wk, L1_gnn_Wv), axis=-1)
    return x

_drawn_inputs = setup_inputs


def setup_inputs(seed=0):
    import zlib

    import numpy as np

    out = dict(_drawn_inputs(seed))
    spreads = {}
    factors = {'L0_gnn_blv': 5.281,
     'L0_gnn_Wgq': 8.0,
     'L0_gnn_Wgk': 8.0,
     'L0_gnn_Wgv': 8.0,
     'L0_gnn_bgv': 8.0,
     'L0_gnn_bev': 8.0}
    for name, (base, spread) in spreads.items():
        noise = np.random.default_rng([zlib.crc32(name.encode()), seed]).standard_normal(out[name].shape)
        drawn = base * np.exp(spread * noise) if base else spread * noise
        out[name] = jnp.asarray(drawn.astype(out[name].dtype))
    for name, factor in factors.items():
        out[name] = (out[name] * factor).astype(out[name].dtype)
    return out
```

```python
import concourse.bass as bass
from concourse import mybir
from contextlib import ExitStack

N = 4096
D = 256
P = 128
NBLK = N // P
NPAIR = NBLK // 2
TILE = 512
NT = N // TILE
LAG = 3
NEXP = 4
EXPW = N // NEXP
EPS = 1e-5
LOWEST = -3.0e38
SHIFT = (34, 60)
EXP_SCALE = (2.0 ** 30, 2.0 ** 60)


def attention_layers(nc, x, adj, mx, wlq, wlk, wlv, blv, wgq, wgk, wgv, bgv, wes, wev, bev, wq, wk, wv, out, x1_dram):
    f32, f32r = mybir.dt.float32, mybir.dt.float32r
    u8, u16, u32 = mybir.dt.uint8, mybir.dt.uint16, mybir.dt.uint32
    ALU, ACT, AX = mybir.AluOpType, mybir.ActivationFunctionType, mybir.AxisListType

    ctx = ExitStack()
    with ctx:
        def sb(name, shape, dt=f32):
            return ctx.enter_context(nc.sbuf_tensor(name, shape, dt))

        def pb(name):
            return ctx.enter_context(nc.psum_tensor(name, [P, 512], f32))

        def sem(name):
            return ctx.enter_context(nc.semaphore(name))

        def by_block(ap):
            return ap.rearrange("(g p b) d -> g b p d", p=P, b=2)

        x_blk, mx_blk, x1_blk, out_blk, adj_blk = (by_block(a) for a in (x, mx, x1_dram, out, adj))
        adj_pairs = adj.bitcast(u16).rearrange("j (g i) -> g j i", g=NPAIR)

        keys = sb("keys", [P, NBLK, 2, D], f32r)
        keysT_hi = sb("keysT_hi", [P, 2, N], f32r)
        keysT_lo = sb("keysT_lo", [P, 2, N], f32r)
        scores = [sb(f"scores{s}", [P, N]) for s in range(2)]
        mask_mem = sb("mask_mem", [P, 4 * N], u8)
        pT_hi = [sb(f"pT_hi{s}", [P, TILE], f32r) for s in range(2)]
        pT_lo = [sb(f"pT_lo{s}", [P, TILE], f32r) for s in range(2)]
        qT_hi = [sb(f"qT_hi{s}", [P, 2, P], f32r) for s in range(2)]
        qT_lo = [sb(f"qT_lo{s}", [P, 2, P], f32r) for s in range(2)]
        res_in = [sb(f"res_in{s}", [P, 2, D]) for s in range(2)]
        mixed = sb("mixed", [P, D])
        turned = sb("turned", [P, 2, P])
        fin = sb("fin", [P, D])
        yrow = [sb(f"yrow{s}", [P, D]) for s in range(2)]
        smax = [sb(f"smax{s}", [P, NT + 2]) for s in range(2)]
        bmax = [sb(f"bmax{s}", [P, 1]) for s in range(2)]
        nbias = [sb(f"nbias{s}", [P, 1]) for s in range(2)]
        sums = [sb(f"sums{s}", [P, NEXP + 2]) for s in range(2)]
        lsum = sb("lsum", [P, 1])
        den = sb("den", [P, 1])
        rden = sb("rden", [P, 1])
        live = sb("live", [P, 1])
        wlive = sb("wlive", [P, 1])
        bst = sb("bst", [P, 6])
        mv = [sb(f"mv{s}", [P, 2]) for s in range(2)]
        veps = sb("veps", [P, 1])
        rstd = [sb(f"rstd{s}", [P, 1]) for s in range(2)]
        minus_half = sb("minus_half", [P, 1])
        ident = sb("ident", [P, P])
        xbarT = sb("xbarT", [P, 2])
        gkT = sb("gkT", [P, 2])
        with ExitStack() as only0:
            def sb0(name, shape, dt=f32):
                return only0.enter_context(nc.sbuf_tensor(name, shape, dt))
            a0 = sb0("a0", [P, 2, D])
            wcat = sb0("wcat", [P, 2, D + 2])
            wlv_sb = sb0("wlv_sb", [P, 2, D])
            gvB = sb0("gvB", [P, D])
            bvB = sb0("bvB", [P, D])
            beB = sb0("beB", [P, D])
        a1_hi = sb("a1_hi", [P, 2, D], f32r)
        a1_lo = sb("a1_lo", [P, 2, D], f32r)
        wvT_sb = sb("wvT_sb", [P, 2, D])
        place_of_layer0 = sb("place_of_layer0", [P, 3 * D + 4])

        inv_rows = [mask_mem[:, s * N:(s + 1) * N] for s in range(2)]
        pair_land = mask_mem[:, 0:2 * N]
        pair_inv = mask_mem[:, 2 * N:4 * N]
        spare = mask_mem[:, :].bitcast(f32)

        def mat(i):
            return spare[:, i * 512:(i + 1) * 512].rearrange("p (h n) -> p h n", h=2)

        wlq_s, wlk_s, wgq_s, wgk_s, wgv_s = (mat(i) for i in range(5))
        wq_s, wk_s, wv_s = (mat(i) for i in (4, 5, 6))
        mx_q, ev, side = ([mat(i)[:, s, :] for s in range(2)] for i in (5, 6, 7))
        stage = [scores[k // 4][:, (k % 4) * 1024:(k % 4 + 1) * 1024] for k in range(8)]
        wlqT, wlkT = res_in
        wgqT = wlkT
        ones = mixed[:, 0:P]
        xbarB = turned
        bgB = fin

        ps_s = [pb(f"ps_s{s}") for s in range(2)]
        ps_t = [pb(f"ps_t{s}") for s in range(2)]
        ps_mix = [pb(f"ps_mix{s}") for s in range(2)]
        ps_a = pb("ps_a")
        ps_b = pb("ps_b")
        ps_x, ps_q = ps_a[:, 0:D], ps_a[:, D:2 * D]

        w_loaded, e_loaded, v_loaded = sem("w_loaded"), sem("e_loaded"), sem("v_loaded")
        const_set, ident_set = sem("const_set"), sem("ident_set")
        pe_setup, act_setup, dve_setup = sem("pe_setup"), sem("act_setup"), sem("dve_setup")
        w1_loaded, pe_setup1, act_setup1, dve_setup1 = sem("w1_loaded"), sem("pe_setup1"), sem("act_setup1"), sem("dve_setup1")

        names = ("stage_loaded hi_nat lo_nat stageT_ps stageT_hi stageT_lo "
                 "adj_loaded "
                 "mxT_ps mxT_sb q_ps q_hi q_lo ev_ps ev_sb gs_sb "
                 "inverted score_ps score_sb max_row bias_set exp_side exp_done pT_ps pT_hi_sb pT_lo_sb mix_ps "
                 "mixlo_sb mixed_sb mixT_ps mixT_sb proj_ps side_step fin_step proj_out veps_set rstd_set y_set").split()

        class Layer:
            pass

        LAYERS = []
        for l in range(2):
            L = Layer()
            L.n = l
            L.s = {n: sem(f"{n}_{l}") for n in names}
            for n in ("mx_loaded", "rows_loaded", "res_loaded", "out_stored"):
                L.s[n] = [sem(f"{n}_{l}_{s}") for s in range(2)]
            LAYERS.append(L)

        FIN_STEPS = (8, 6)

        def key_rows(src_blk, k):
            src = (x if src_blk == 0 else x1_dram)
            return src.rearrange("(g p b) d -> p g (b d)", p=P, b=2)[:, 2 * k:2 * k + 2, :]

        def steps(engine, L, step):
            for R in range(4):
                step(R, R % 2, R)
            with engine.Fori(2, NPAIR - 1) as g:
                L.g = g
                for s in range(2):
                    step(2 * g + s, s, 4 + s)
            for R in range(NBLK - 2, NBLK + 3):
                step(R, R % 2, R)

        def nth(L, R, s, off):
            return (R + off) // 2 if isinstance(R, int) else L.g + (s + off) // 2

        def wait_apart(engine, semaphore, value):
            if not isinstance(value, int):
                value = engine.snap(engine.to_reg(value))
                engine.wait_ge(ident_set, 2)
            engine.wait_ge(semaphore, value)

        PE_SETUP = 8

        block = ctx.enter_context(nc.Block())

        @block.sync
        def _(sp):
            S0 = LAYERS[0].s
            for t, w in ((wlq_s, wlq), (wlk_s, wlk), (wgq_s, wgq), (wgk_s, wgk), (wgv_s, wgv)):
                sp.dma_start(t, w.rearrange("(h p) n -> p h n", h=2)).then_inc(w_loaded, 16)
            for k in range(8):
                sp.dma_start(stage[k].rearrange("p (g d) -> p g d", g=2), key_rows(0, k)).then_inc(S0["stage_loaded"], 16)
            sp.dma_start(wcat[:, :, 0:D], wev.rearrange("(h p) n -> p h n", h=2)).then_inc(e_loaded, 16)
            sp.dma_start(wcat[:, :, D + 1:D + 2], wes.rearrange("(h p) n -> p h n", h=2),
                         allow_slow_non_contiguous=True).then_inc(e_loaded, 16)
            for t, b in ((bvB, blv), (beB, bev), (bgB, bgv)):
                sp.dma_start(t[:, :], b.partition_broadcast(P)).then_inc(e_loaded, 16)
            sp.dma_start(wlv_sb[:, :, :], wlv.rearrange("(h p) n -> p h n", h=2)).then_inc(v_loaded, 16)

            for L in LAYERS:
                S = L.s
                if L.n == 1:
                    for s in range(2):
                        sp.wait_ge(LAYERS[0].s["out_stored"][s], 16 * NPAIR)
                    for k in range(8):
                        sp.dma_start(stage[k].rearrange("p (g d) -> p g d", g=2), key_rows(1, k)).then_inc(S["stage_loaded"], 16)
                    for t, w in ((wq_s, wq), (wk_s, wk), (wv_s, wv)):
                        sp.dma_start(t, w.rearrange("(h p) n -> p h n", h=2)).then_inc(w1_loaded, 16)
                    sp.dma_start_transpose(pair_land.bitcast(u16).rearrange("p (o j) -> p o j", o=1),
                                           adj_pairs[0, :, :]).then_inc(S["adj_loaded"], 16)
                else:
                    for R in (0, 1):
                        sp.dma_start(mx_q[R], mx_blk[0, R, :, :]).then_inc(S["mx_loaded"][R], 16)
                    sp.wait_ge(pe_setup, PE_SETUP)
                    sp.dma_start(inv_rows[0], adj_blk[0, 0, :, :]).then_inc(S["rows_loaded"][0], 16)

                def step(R, s, R0):
                    g = (R - s) // 2 if isinstance(R, int) else None
                    def blk(view, off):
                        b = (s + off) % 2
                        if isinstance(R, int):
                            return view[(R + off) // 2, b, :, :]
                        return view[bass.ds(L.g + (s + off - b) // 2, 1), b, :, :].rearrange("o p d -> (o p) d")
                    if L.n == 0:
                        if R0 + 1 < NBLK:
                            if R0 >= 1:
                                wait_apart(sp, S["score_sb"], 8 * R)
                            sp.dma_start(inv_rows[1 - s], blk(adj_blk, 1)).then_inc(S["rows_loaded"][1 - s], 16)
                        if R0 + 2 < NBLK:
                            wait_apart(sp, S["mxT_ps"], R + 1)
                            sp.dma_start(mx_q[s], blk(mx_blk, 2)).then_inc(S["mx_loaded"][s], 16)
                    elif s == 0 and R0 + 2 < NBLK:
                        wait_apart(sp, S["inverted"], 4 * R + 8)
                        nxt = adj_pairs[R // 2 + 1, :, :] if isinstance(R, int) else \
                            adj_pairs[bass.ds(L.g + 1, 1), :, :].rearrange("o j i -> (o j) i")
                        sp.dma_start_transpose(pair_land.bitcast(u16).rearrange("p (o j) -> p o j", o=1),
                                               nxt).then_inc(S["adj_loaded"], 16)
                    if 1 <= R0 <= NBLK:
                        if R0 >= 3:
                            wait_apart(sp, S["fin_step"], FIN_STEPS[L.n] * (R - 2))
                        src = x_blk if L.n == 0 else x1_blk
                        sp.dma_start(res_in[1 - s][:, 0, :], blk(src, -1)).then_inc(S["res_loaded"][1 - s], 16)
                        if L.n == 0:
                            sp.dma_start(res_in[1 - s][:, 1, :], blk(mx_blk, -1)).then_inc(S["res_loaded"][1 - s], 16)
                    if R0 >= 3:
                        wait_apart(sp, S["y_set"], R - 2)
                        dst = x1_blk if L.n == 0 else out_blk
                        sp.dma_start(blk(dst, -3), yrow[1 - s][:, :]).then_inc(S["out_stored"][1 - s], 16)

                steps(sp, L, step)
            for s in range(2):
                sp.wait_ge(LAYERS[1].s["out_stored"][s], 16 * NPAIR)

        @block.tensor
        def _(pe):
            mm, tr = nc.tensor.matmul, nc.tensor.transpose

            def build_keys(L):
                S = L.s
                for k in range(8):
                    pe.wait_ge(S["stage_loaded"], 16 * 8)
                    if k >= 2:
                        pe.wait_ge(S["stageT_lo"], 2 * (k - 1))
                    for h in range(2):
                        bank = (ps_t, ps_s)[k % 2][h]
                        for j in range(4):
                            last = tr(bank[:, j * P:(j + 1) * P], stage[k][:, j * D + h * P:j * D + (h + 1) * P], ident[:, :])
                        last.then_inc(S["stageT_ps"], 1)

            def transpose_weights(bank_of, w, done):
                for h in range(2):
                    for r in range(2):
                        last = tr(bank_of[:, h * D + r * P:h * D + (r + 1) * P], w[:, r, h * P:(h + 1) * P], ident[:, :])
                last.then_inc(done, 1)

            def product(dst, lhs, rhs, done):
                for m in range(2):
                    for h in range(2):
                        last = mm(dst(m), lhs[:, h, m * P:(m + 1) * P], rhs(h), start=(h == 0), stop=(h == 1))
                last.then_inc(done, 1)

            pe.wait_ge(ident_set, 2)
            pe.wait_ge(w_loaded, 16 * 5)
            transpose_weights(ps_mix[0], wlq_s, pe_setup)
            transpose_weights(ps_mix[1], wlk_s, pe_setup)
            pe.wait_ge(dve_setup, 2)
            product(lambda m: ps_b[:, m * D:(m + 1) * D], wlqT, lambda h: wlkT[:, h, :], pe_setup)
            transpose_weights(ps_mix[0], wgq_s, pe_setup)
            pe.wait_ge(act_setup, 1)
            pe.wait_ge(const_set, 2)
            pe.wait_ge(LAYERS[0].s["stage_loaded"], 16 * 8)
            for h in range(2):
                bank = (ps_a, ps_b)[h]
                for j in range(NBLK):
                    c = (j % 4) * D + h * P
                    last = mm(bank[:, 0:1], stage[j // 4][:, c:c + P], ones[:, 0:1], start=(j == 0), stop=(j == NBLK - 1))
            last.then_inc(pe_setup, 1)
            pe.wait_ge(dve_setup, 7)
            product(lambda m: ps_a[:, m:m + 1], wgk_s, lambda h: xbarT[:, h:h + 1], pe_setup)
            for h in range(2):
                last = mm(ps_b[:, 0:D], xbarB[:, h, :], wgv_s[:, h, :], start=(h == 0), stop=(h == 1))
            last.then_inc(pe_setup, 1)
            pe.wait_ge(dve_setup, 8)
            product(lambda m: ps_mix[0][:, m:m + 1], wgqT, lambda h: gkT[:, h:h + 1], pe_setup)

            for L in LAYERS:
                S = L.s
                if L.n == 1:
                    pe.wait_ge(w1_loaded, 16 * 3)
                    product(lambda m: ps_b[:, m * D:(m + 1) * D], wq_s, lambda h: wk_s[:, h, :], pe_setup1)
                    transpose_weights(ps_mix[0], wv_s, pe_setup1)
                build_keys(L)

                def prep_mxT(nxt, s, R0, seen):
                    pe.wait_ge(S["mx_loaded"][s], 16 * seen + 16)
                    if R0 >= 0:
                        pe.wait_ge(S["q_lo"], nxt)
                    if R0 >= 3:
                        pe.wait_ge(S["mixT_sb"], nxt - 3)
                    if R0 < 0:
                        pe.wait_ge(dve_setup, 11)
                    for h in range(2):
                        last = tr(ps_a[:, h * P:(h + 1) * P], mx_q[s][:, h * P:(h + 1) * P], ident[:, :])
                    last.then_inc(S["mxT_ps"], 1)

                def prep_q(nxt, s, R0, g2):
                    if R0 >= 0:
                        pe.wait_ge(S["q_lo"], nxt)
                    if L.n == 1 and R0 >= 3:
                        pe.wait_ge(S["mixT_sb"], nxt - 3)
                    if L.n == 0:
                        pe.wait_ge(S["mxT_sb"], nxt + 1)
                        for m in range(2):
                            for h in range(2):
                                last = mm(ps_a[:, D + m * P:D + (m + 1) * P], a0[:, h, m * P:(m + 1) * P], turned[:, h, :],
                                          start=(h == 0), stop=(h == 1))
                    else:
                        for m in range(2):
                            n = 0
                            for h in range(2):
                                def cols(t):
                                    v = t[:, h, :].rearrange("q (g p b) -> q g p b", p=P, b=2)
                                    if isinstance(g2, int):
                                        return v[:, g2, :, s]
                                    return v[:, bass.ds(g2, 1), :, s].rearrange("q o p -> q (o p)")
                                for a, b in ((a1_hi, keysT_hi), (a1_hi, keysT_lo), (a1_lo, keysT_hi)):
                                    last = mm(ps_a[:, D + m * P:D + (m + 1) * P], a[:, h, m * P:(m + 1) * P], cols(b),
                                              start=(n == 0), stop=(n == 5))
                                    n += 1
                    last.then_inc(S["q_ps"], 1)

                def prep_ev(nxt, R0):
                    if R0 >= 3:
                        pe.wait_ge(S["proj_out"], nxt - 3)
                    for h in range(2):
                        last = mm(ps_b[:, 0:D + 2], turned[:, h, :], wcat[:, h, :], start=(h == 0), stop=(h == 1))
                    last.then_inc(S["ev_ps"], 1)

                if L.n == 0:
                    prep_mxT(0, 0, -1, 0)
                    prep_q(0, 0, -1, 0)
                    prep_ev(0, -1)
                    pe.wait_ge(v_loaded, 16)
                else:
                    pe.wait_ge(S["stageT_lo"], 16)
                    pe.wait_ge(dve_setup1, 1)
                    pe.wait_ge(act_setup1, 2)
                    prep_q(0, 0, -1, 0)
                pe.wait_ge(S["stageT_lo"], 16)
                pe.wait_ge(S["lo_nat"], 8)

                def step(R, s, R0):
                    for c in range(NT):
                        nxt = R0 + 1 < NBLK
                        if L.n == 0 and nxt and c == 0:
                            prep_mxT(R + 1, 1 - s, R0, nth(L, R, s, 1))
                        if nxt and c == 2:
                            prep_q(R + 1, 1 - s, R0, nth(L, R, s, 1))
                        if L.n == 0 and nxt and c == 3:
                            prep_ev(R + 1, R0)
                        if 0 <= R0 - 2 < NBLK and c == 4:
                            pe.wait_ge(S["mixed_sb"], R - 1)
                            if nxt:
                                pe.wait_ge(S["q_lo"], R + 2)
                            for h in range(2):
                                last = tr(ps_a[:, h * P:(h + 1) * P], mixed[:, h * P:(h + 1) * P], ident[:, :])
                            last.then_inc(S["mixT_ps"], 1)
                        if 0 <= R0 - 2 < NBLK and c == 6:
                            pe.wait_ge(S["mixT_sb"], R - 1)
                            if L.n == 0 and nxt:
                                pe.wait_ge(S["ev_sb"], R + 2)
                                pe.wait_ge(S["gs_sb"], R + 2)
                            if L.n == 1 and R0 >= 3:
                                pe.wait_ge(S["proj_out"], R - 2)
                            w = wlv_sb if L.n == 0 else wvT_sb
                            for h in range(2):
                                last = mm(ps_b[:, 0:D], turned[:, h, :], w[:, h, :], start=(h == 0), stop=(h == 1))
                            last.then_inc(S["proj_ps"], 1)
                        back = 1 if c >= LAG - 1 else 2
                        cc = (c - (LAG - 1)) % NT
                        if 0 <= R0 - back < NBLK:
                            B = R - back
                            pe.wait_ge(S["exp_done"], NEXP * B + (cc * TILE) // EXPW + 1)
                            if R0 - back > 0 or cc >= 2:
                                pe.wait_ge(S["pT_lo_sb"], 8 * B + cc - 1)
                            sc = scores[(s + back) % 2][:, cc * TILE:(cc + 1) * TILE].rearrange("i (g p b) -> i g b p", p=P, b=2)
                            for j in range(4):
                                last = tr(ps_t[cc % 2][:, j * P:(j + 1) * P], sc[:, j // 2, j % 2, :], ident[:, :])
                            last.then_inc(S["pT_ps"], 1)
                        if R0 < NBLK:
                            if c == 0:
                                pe.wait_ge(S["q_lo"], R + 1)
                            if R0 > 0 or c >= 2:
                                pe.wait_ge(S["score_sb"], 8 * R + c - 1)
                            n = 0
                            for h in range(2):
                                for q, k in ((qT_hi, keysT_hi), (qT_hi, keysT_lo), (qT_lo, keysT_hi)):
                                    last = mm(ps_s[c % 2][:, :], q[s][:, h, :], k[:, h, c * TILE:(c + 1) * TILE],
                                              start=(n == 0), stop=(n == 5))
                                    n += 1
                            last.then_inc(S["score_ps"], 1)
                        back = 1 if c >= LAG else 2
                        cc = (c - LAG) % NT
                        if 0 <= R0 - back < NBLK:
                            B = R - back
                            pe.wait_ge(S["pT_lo_sb"], 8 * B + cc + 1)
                            acc = ps_mix[(s + back) % 2]
                            if cc == 0 and R0 - back >= 2:
                                pe.wait_ge(S["mixed_sb"], B - 1)
                            for j in range(4):
                                kb = 4 * cc + j
                                def hi():
                                    return mm(acc[:, :], pT_hi[cc % 2][:, j * P:(j + 1) * P],
                                              keys[:, kb, :, :].rearrange("p t d -> p (t d)"),
                                              start=(kb == 0), stop=(kb == NBLK - 1), skip_group_check=True)
                                def lo():
                                    return mm(acc[:, 0:D], pT_lo[cc % 2][:, j * P:(j + 1) * P], keys[:, kb, 0, :],
                                              start=False, stop=False, skip_group_check=True)
                                for part in ((hi, lo) if kb == 0 else (lo, hi)):
                                    last = part()
                            last.then_inc(S["mix_ps"], 1)

                steps(pe, L, step)

        @block.scalar
        def _(act):
            A = nc.scalar.activation

            def build_keys(L):
                S = L.s
                for k in range(8):
                    act.wait_ge(S["stage_loaded"], 16 * 8)
                    A(keys[:, 4 * k:4 * k + 4, 0, :], stage[k].rearrange("p (j d) -> p j d", d=D), ACT.Copy).then_inc(S["hi_nat"], 1)
                    for h in range(2):
                        act.wait_ge(S["stageT_ps"], 2 * k + h + 1)
                        bank = (ps_t, ps_s)[k % 2][h]
                        A(keysT_hi[:, h, k * TILE:(k + 1) * TILE].rearrange("q (g p b) -> q g b p", p=P, b=2),
                          bank[:, :].rearrange("q (g b p) -> q g b p", g=2, b=2), ACT.Copy).then_inc(S["stageT_hi"], 1)

            def halves(t):
                return t.rearrange("p (h n) -> p h n", h=2)

            act.wait_ge(pe_setup, 3)
            A(a0[:, :, :], halves(ps_b[:, :]), ACT.Copy, scale=2.0 ** -SHIFT[0]).then_inc(act_setup, 1)

            for L in LAYERS:
                S = L.s
                if L.n == 1:
                    act.wait_ge(pe_setup1, 1)
                    A(a1_hi[:, :, :], halves(ps_b[:, :]), ACT.Copy, scale=2.0 ** -SHIFT[1]).then_inc(act_setup1, 1)
                    act.wait_ge(pe_setup1, 2)
                    A(wvT_sb[:, :, :], halves(ps_mix[0][:, :]), ACT.Copy).then_inc(act_setup1, 1)
                build_keys(L)

                def prep_mxT(nxt, R0):
                    act.wait_ge(S["mxT_ps"], nxt + 1)
                    if R0 >= 0:
                        act.wait_ge(S["ev_ps"], nxt)
                    if R0 >= 3:
                        act.wait_ge(S["proj_ps"], nxt - 3)
                    A(turned[:, :, :], ps_x.rearrange("p (h n) -> p h n", h=2), ACT.Copy).then_inc(S["mxT_sb"], 1)

                def prep_q(nxt, s):
                    act.wait_ge(S["q_ps"], nxt + 1)
                    A(qT_hi[s][:, :, :], ps_q.rearrange("p (h n) -> p h n", h=2), ACT.Copy).then_inc(S["q_hi"], 1)

                def prep_ev(nxt, s, R0):
                    act.wait_ge(S["ev_ps"], nxt + 1)
                    if R0 >= 1:
                        act.wait_ge(S["side_step"], 4 * (nxt - 1))
                    A(ev[s], ps_b[:, 0:D], ACT.Copy).then_inc(S["ev_sb"], 1)

                if L.n == 0:
                    prep_mxT(0, -1)
                prep_q(0, 0)
                if L.n == 0:
                    prep_ev(0, 0, -1)

                def step(R, s, R0):
                    for c in range(NT):
                        nxt = R0 + 1 < NBLK
                        if L.n == 0 and nxt and c == 0:
                            prep_mxT(R + 1, R0)
                        back = 1 if c >= LAG - 1 else 2
                        cc = (c - (LAG - 1)) % NT
                        if 0 <= R0 - back < NBLK:
                            B = R - back
                            act.wait_ge(S["pT_ps"], 8 * B + cc + 1)
                            if R0 - back > 0 or cc >= 2:
                                act.wait_ge(S["mix_ps"], 8 * B + cc - 1)
                            A(pT_hi[cc % 2][:, :], ps_t[cc % 2][:, :], ACT.Copy).then_inc(S["pT_hi_sb"], 1)
                        if 0 <= R0 - 1 < NBLK and c % 2 == 0:
                            e = c // 2
                            o = 1 - s
                            if c == 0:
                                act.wait_ge(S["bias_set"], R)
                                if R0 - 1 >= 2:
                                    act.wait_ge(S["fin_step"], FIN_STEPS[L.n] * (R - 2))
                                if L.n == 0:
                                    A(sums[o][:, NEXP:NEXP + 2], smax[o][:, NT:NT + 2], ACT.Exp, bias=nbias[o][:, :],
                                      scale=EXP_SCALE[0]).then_inc(S["exp_side"], 1)
                            sc = scores[o][:, e * EXPW:(e + 1) * EXPW]
                            A(sc, sc, ACT.Exp, bias=nbias[o][:, :], scale=EXP_SCALE[L.n],
                              accum_out=sums[o][:, e:e + 1]).then_inc(S["exp_done"], 1)
                        if nxt and c == 2:
                            prep_q(R + 1, 1 - s)
                        if 0 <= R0 - 2 < NBLK and c == 3:
                            act.wait_ge(S["mix_ps"], 8 * (R - 1))
                            if R0 - 2 >= 1:
                                act.wait_ge(S["mixT_ps"], R - 2)
                            A(mixed[:, :], ps_mix[s][:, D:2 * D], ACT.Copy).then_inc(S["mixlo_sb"], 1)
                        if L.n == 0 and nxt and c == 4:
                            prep_ev(R + 1, 1 - s, R0)
                        if 0 <= R0 - 2 < NBLK and c == 4:
                            act.wait_ge(S["mixT_ps"], R - 1)
                            if R0 - 2 >= 1:
                                act.wait_ge(S["proj_ps"], R - 2)
                            A(turned[:, :, :], ps_x.rearrange("p (h n) -> p h n", h=2), ACT.Copy).then_inc(S["mixT_sb"], 1)

                steps(act, L, step)

        @block.vector
        def _(dve):
            V = nc.vector

            def build_keys(L):
                S = L.s
                for k in range(8):
                    dve.wait_ge(S["hi_nat"], k + 1)
                    V.tensor_tensor(keys[:, 4 * k:4 * k + 4, 1, :], stage[k].rearrange("p (j d) -> p j d", d=D),
                                    keys[:, 4 * k:4 * k + 4, 0, :].bitcast(f32), ALU.subtract).then_inc(S["lo_nat"], 1)
                    for h in range(2):
                        dve.wait_ge(S["stageT_hi"], 2 * k + h + 1)
                        bank = (ps_t, ps_s)[k % 2][h]
                        dst = [t[:, h, k * TILE:(k + 1) * TILE].rearrange("q (g p b) -> q g b p", p=P, b=2)
                               for t in (keysT_lo, keysT_hi)]
                        V.tensor_tensor(dst[0], bank[:, :].rearrange("q (g b p) -> q g b p", g=2, b=2),
                                        dst[1].bitcast(f32), ALU.subtract).then_inc(S["stageT_lo"], 1)

            def halves(t):
                return t.rearrange("p (h n) -> p h n", h=2)

            dve.wait_ge(pe_setup, 1)
            V.tensor_copy(wlqT[:, :, :], halves(ps_mix[0][:, :])).then_inc(dve_setup, 1)
            dve.wait_ge(pe_setup, 2)
            V.tensor_copy(wlkT[:, :, :], halves(ps_mix[1][:, :])).then_inc(dve_setup, 1)
            dve.wait_ge(pe_setup, 4)
            V.tensor_copy(wgqT[:, :, :], halves(ps_mix[0][:, :])).then_inc(dve_setup, 1)
            dve.wait_ge(pe_setup, 5)
            for h in range(2):
                V.tensor_scalar(xbarT[:, h:h + 1], (ps_a, ps_b)[h][:, 0:1], 1.0 / N, None, ALU.mult).then_inc(dve_setup, 1)
            dve.wait_ge(dve_setup, 5)
            dve.wait_ge(const_set, 2)
            for h in range(2):
                V.tensor_scalar(xbarB[:, h, :], ones[:, :], xbarT[:, h:h + 1], None, ALU.mult).then_inc(dve_setup, 1)
            dve.wait_ge(pe_setup, 6)
            V.tensor_copy(gkT[:, :], ps_a[:, 0:2]).then_inc(dve_setup, 1)
            dve.wait_ge(pe_setup, 7)
            dve.wait_ge(e_loaded, 16 * 5)
            V.tensor_tensor(gvB[:, :], ps_b[:, 0:D], bgB[:, :], ALU.add).then_inc(dve_setup, 1)
            self_col = wcat[:, :, D + 1:D + 2].rearrange("p h o -> p (h o)")
            V.tensor_scalar(self_col, self_col, 1.0 / EXP_SCALE[0], None, ALU.mult).then_inc(dve_setup, 1)
            dve.wait_ge(pe_setup, 8)
            V.tensor_scalar(wcat[:, :, D:D + 1].rearrange("p h o -> p (h o)"), ps_mix[0][:, 0:2], 2.0 ** -SHIFT[0], None,
                            ALU.mult).then_inc(dve_setup, 1)

            for L in LAYERS:
                S = L.s
                if L.n == 1:
                    dve.wait_ge(act_setup1, 1)
                    V.scalar_tensor_tensor(a1_lo[:, :, :].rearrange("p h n -> p (h n)"), ps_b[:, :], 2.0 ** -SHIFT[1],
                                           a1_hi[:, :, :].rearrange("p h n -> p (h n)").bitcast(f32),
                                           ALU.mult, ALU.subtract).then_inc(dve_setup1, 1)
                build_keys(L)
                NM = NT + 2 if L.n == 0 else NT

                def prep_q_lo(nxt, s):
                    dve.wait_ge(S["q_hi"], nxt + 1)
                    V.tensor_tensor(qT_lo[s][:, :, :], ps_q.rearrange("p (h n) -> p h n", h=2),
                                    qT_hi[s][:, :, :].bitcast(f32), ALU.subtract).then_inc(S["q_lo"], 1)

                def prep_gs(nxt, s, R0):
                    dve.wait_ge(S["ev_sb"], nxt + 1)
                    if R0 >= 1:
                        dve.wait_ge(S["exp_side"], nxt - 1)
                    V.tensor_copy(smax[s][:, NT:NT + 2], ps_b[:, D:D + 2]).then_inc(S["gs_sb"], 1)

                def invert_rows(nxt, s, seen):
                    dve.wait_ge(S["rows_loaded"][s], 16 * seen + 16)
                    w = inv_rows[s].bitcast(u32)
                    V.tensor_single_scalar(w, w, 0x01010101, op=ALU.bitwise_xor).then_inc(S["inverted"], 1)

                def invert_pair(c):
                    r = slice(c * 2 * TILE, (c + 1) * 2 * TILE)
                    V.tensor_single_scalar(pair_inv[:, r].bitcast(u32), pair_land[:, r].bitcast(u32), 0x01010101,
                                           op=ALU.bitwise_xor).then_inc(S["inverted"], 1)

                if L.n == 0:
                    prep_q_lo(0, 0)
                    prep_gs(0, 0, -1)
                    invert_rows(0, 0, 0)
                else:
                    prep_q_lo(0, 0)
                    dve.wait_ge(S["adj_loaded"], 16)
                    dve.wait_ge(pe_setup1, 2)
                    for c in range(NT):
                        invert_pair(c)

                def step(R, s, R0):
                    fin_ok = 0 <= R0 - 2 < NBLK
                    F = R - 2
                    NF = FIN_STEPS[L.n]
                    for c in range(NT):
                        nxt = R0 + 1 < NBLK
                        if c == 1 and R0 - 3 >= 0:
                            dve.wait_ge(S["rstd_set"], R - 2)
                            V.tensor_scalar(yrow[1 - s][:, :], yrow[1 - s][:, :], mv[1 - s][:, 0:1], rstd[1 - s][:, :],
                                            ALU.subtract, ALU.mult).then_inc(S["y_set"], 1)
                        back = 1 if c >= LAG - 1 else 2
                        cc = (c - (LAG - 1)) % NT
                        if 0 <= R0 - back < NBLK:
                            B = R - back
                            dve.wait_ge(S["pT_hi_sb"], 8 * B + cc + 1)
                            V.tensor_tensor(pT_lo[cc % 2][:, :], ps_t[cc % 2][:, :], pT_hi[cc % 2][:, :].bitcast(f32),
                                            ALU.subtract).then_inc(S["pT_lo_sb"], 1)
                        if nxt and c == 3:
                            prep_q_lo(R + 1, 1 - s)
                        if L.n == 0 and nxt and c == 4:
                            prep_gs(R + 1, 1 - s, R0)
                        if L.n == 0 and nxt and c == 5:
                            invert_rows(R + 1, 1 - s, nth(L, R, s, 1))
                        if R0 < NBLK:
                            if L.n == 0:
                                if c == 0:
                                    dve.wait_ge(S["inverted"], R + 1)
                                inv = inv_rows[s][:, c * TILE:(c + 1) * TILE]
                            else:
                                if s == 0:
                                    dve.wait_ge(S["inverted"], 4 * R + c + 1)
                                inv = pair_inv.rearrange("p (j b) -> p j b", b=2)[:, c * TILE:(c + 1) * TILE, s]
                            wait_apart(dve, S["score_ps"], 8 * R + c + 1)
                            V.tensor_tensor_reduce(out=scores[s][:, c * TILE:(c + 1) * TILE], in0=ps_s[c % 2][:, :], in1=inv,
                                                   scale=1.0, scalar=LOWEST, op0=ALU.subtract, op1=ALU.max,
                                                   accum_out=smax[s][:, c:c + 1]).then_inc(S["score_sb"], 1)
                            if L.n == 1 and s == 1 and nxt:
                                if c == 0:
                                    dve.wait_ge(S["adj_loaded"], 8 * R + 24)
                                dve.wait_ge(S["score_sb"], 8 * R + c + 1)
                                invert_pair(c)
                        if fin_ok:
                            if c == 3:
                                dve.wait_ge(S["mixlo_sb"], R - 1)
                                V.tensor_tensor(mixed[:, :], ps_mix[s][:, 0:D], mixed[:, :], ALU.add).then_inc(S["mixed_sb"], 1)
                            fs = S["fin_step"]
                            if c == 5:
                                dve.wait_ge(S["exp_done"], NEXP * (R - 1))
                                if L.n == 0:
                                    V.reduce_sum(lsum[:, :], sums[s][:, 0:NEXP], AX.X).then_inc(fs, 1)
                                    V.reduce_sum(den[:, :], sums[s][:, 0:NEXP + 2], AX.X).then_inc(fs, 1)
                                    dve.wait_ge(fs, NF * F + 2)
                                    V.reciprocal(rden[:, :], den[:, :]).then_inc(fs, 1)
                                    dve.wait_ge(S["side_step"], 4 * (R - 1))
                                    V.scalar_tensor_tensor(fin[:, :], bvB[:, :], lsum[:, :], side[s], ALU.mult, ALU.add).then_inc(fs, 1)
                                else:
                                    V.tensor_scalar(live[:, :], bmax[s][:, :], -0.5, None, ALU.is_gt).then_inc(fs, 1)
                                    V.reduce_sum(den[:, :], sums[s][:, 0:NEXP], AX.X).then_inc(fs, 1)
                                    dve.wait_ge(fs, NF * F + 2)
                                    V.reciprocal(rden[:, :], den[:, :]).then_inc(fs, 1)
                                    dve.wait_ge(fs, NF * F + 3)
                                    V.tensor_tensor(wlive[:, :], rden[:, :], live[:, :], ALU.mult).then_inc(fs, 1)
                        if R0 < NBLK and c == 7:
                            dve.wait_ge(S["score_sb"], 8 * R + 8)
                            if L.n == 0:
                                dve.wait_ge(S["gs_sb"], R + 1)
                            V.reduce_max(bmax[s][:, :], smax[s][:, 0:NM], AX.X).then_inc(S["max_row"], 1)
                            dve.wait_ge(S["max_row"], R + 1)
                            if R0 - 2 >= 0:
                                dve.wait_ge(S["exp_done"], NEXP * (R - 1))
                            V.tensor_scalar(nbias[s][:, :], bmax[s][:, :], -EXP_SCALE[L.n], None, ALU.mult).then_inc(S["bias_set"], 1)
                        if fin_ok:
                            if c == 7:
                                dve.wait_ge(S["proj_ps"], R - 1)
                                dve.wait_ge(fs, NF * F + 4)
                                if R0 - 2 >= 2:
                                    dve.wait_ge(S["out_stored"][s], 16 * nth(L, R, s, -2))
                                if L.n == 0:
                                    dve.wait_ge(S["res_loaded"][s], 32 * nth(L, R, s, 0))
                                    V.tensor_tensor(fin[:, :], ps_b[:, 0:D], fin[:, :], ALU.add).then_inc(S["proj_out"], 1)
                                    dve.wait_ge(S["proj_out"], R - 1)
                                    V.scalar_tensor_tensor(fin[:, :], fin[:, :], rden[:, :], res_in[s][:, 1, :],
                                                           ALU.mult, ALU.max).then_inc(fs, 1)
                                    dve.wait_ge(fs, NF * F + 5)
                                    V.tensor_tensor(yrow[s][:, :], fin[:, :], res_in[s][:, 0, :], ALU.add).then_inc(fs, 1)
                                    dve.wait_ge(fs, NF * F + 6)
                                else:
                                    dve.wait_ge(S["res_loaded"][s], 16 * nth(L, R, s, 0))
                                    V.scalar_tensor_tensor(yrow[s][:, :], ps_b[:, 0:D], wlive[:, :], res_in[s][:, 0, :],
                                                           ALU.mult, ALU.add).then_inc(S["proj_out"], 1)
                                    dve.wait_ge(S["proj_out"], R - 1)
                                V.bn_stats(bst[:, :], yrow[s][:, :]).then_inc(fs, 1)
                                wait_apart(dve, fs, NF * (F + 1) - 1)
                                V.bn_aggr(mv[s][:, :], bst[:, :]).then_inc(fs, 1)

                steps(dve, L, step)

        @block.gpsimd
        def _(pool):
            G = nc.gpsimd
            G.memset(ident[:, :], 0.0).then_inc(ident_set, 1)
            pool.wait_ge(ident_set, 1)
            G.affine_select(out=ident[:, :], in_=ident[:, :], compare_op=ALU.not_equal, fill=1.0, base=0,
                            pattern=[[-1, P]], channel_multiplier=1).then_inc(ident_set, 1)
            G.memset(minus_half[:, :], -0.5).then_inc(const_set, 1)
            G.memset(ones[:, :], 1.0).then_inc(const_set, 1)
            for L in LAYERS:
                S = L.s
                NF = FIN_STEPS[L.n]

                def step(R, s, R0):
                    if L.n == 0 and 0 <= R0 - 1 < NBLK:
                        o = 1 - s
                        ss = S["side_step"]
                        if R0 == 1:
                            pool.wait_ge(e_loaded, 16 * 5)
                            pool.wait_ge(dve_setup, 9)
                        pool.wait_ge(S["ev_sb"], R)
                        G.tensor_tensor(ev[o], ev[o], beB[:, :], ALU.add).then_inc(ss, 1)
                        wait_apart(pool, S["exp_side"], R)
                        wait_apart(pool, ss, 4 * R - 3)
                        G.tensor_scalar(ev[o], ev[o], sums[o][:, NEXP + 1:NEXP + 2], None, ALU.mult).then_inc(ss, 1)
                        if R0 >= 3:
                            wait_apart(pool, S["fin_step"], NF * (R - 2))
                        G.tensor_scalar(side[o], gvB[:, :], sums[o][:, NEXP:NEXP + 1], None, ALU.mult).then_inc(ss, 1)
                        pool.wait_ge(ss, 4 * R - 1)
                        G.tensor_tensor(side[o], side[o], ev[o], ALU.add).then_inc(ss, 1)
                    if 0 <= R0 - 2 < NBLK:
                        if R0 == 2:
                            wait_apart(pool, const_set, 2)
                        wait_apart(pool, S["fin_step"], NF * (R - 1))
                        G.tensor_scalar(veps[:, :], mv[s][:, 1:2], EPS, None, ALU.add).then_inc(S["veps_set"], 1)
                        pool.wait_ge(S["veps_set"], R - 1)
                        G.tensor_tensor(rstd[s][:, :], veps[:, :], minus_half[:, :], ALU.pow).then_inc(S["rstd_set"], 1)

                steps(pool, L, step)
    return nc


_INS = ["x", "adj", "L0_gnn_masked_x", "L0_gnn_Wlq", "L0_gnn_Wlk", "L0_gnn_Wlv", "L0_gnn_blv", "L0_gnn_Wgq", "L0_gnn_Wgk",
        "L0_gnn_Wgv", "L0_gnn_bgv", "L0_gnn_Wes", "L0_gnn_Wev", "L0_gnn_bev", "L1_gnn_Wq", "L1_gnn_Wk", "L1_gnn_Wv"]


def kernel(**inputs):
    import numpy as _np
    import concourse.bacc as _bacc
    from concourse import mybir as _mybir
    from concourse.bass_utils import run_bass_kernel_spmd as _run

    nc = _bacc.Bacc("TRN2", target_bir_lowering=False, num_devices=1)
    arrays, args = {}, []
    for name in _INS:
        a = _np.ascontiguousarray(inputs[name])
        arrays[f"in_{name}"] = a
        args.append(nc.dram_tensor(f"in_{name}", a.shape, _mybir.dt.from_np(a.dtype), kind="ExternalInput").ap())
    out = nc.dram_tensor("out_0", (N, D), _mybir.dt.float32, kind="ExternalOutput").ap()
    x1_dram = nc.dram_tensor("x1_dram", (N, D), _mybir.dt.float32).ap()
    attention_layers(nc, *args, out, x1_dram)
    r = _run(nc, [arrays], core_ids=[0])
    return r.results[0]["out_0"]
```
